# Optimizing a Trainium2 kernel written in Bass

```python
import numpy as np
import jax
import jax.numpy as jnp

def _softmax(x, axis=-1):
    return jax.nn.softmax(x, axis=axis)

def _gelu(x):
    return jax.nn.gelu(x, approximate=True)

def _silu(x):
    return jax.nn.silu(x)

def _sigmoid(x):
    return jax.nn.sigmoid(x)

def _layernorm(x, axis=-1, eps=1e-05):
    m = jnp.mean(x, axis=axis, keepdims=True)
    v = jnp.var(x, axis=axis, keepdims=True)
    return (x - m) / jnp.sqrt(v + eps)

def _scatter_add(tgt, idx, src, axis=0):
    return tgt.at[idx].add(src)

def _segment_sum(src, seg, n):
    return jax.ops.segment_sum(src, seg, n)
kernel_name = 'mk_dlrm_tower_d1_rec_r8_90fe55'

def setup_inputs(seed: int=0):
    np.random.seed(seed)
    _w = jnp.asarray

    def _rec_inputs():
        import jax
        import jax.numpy as jnp
        _tk = jax.random.key(seed)
        ids = jnp.stack([jax.random.randint(jax.random.fold_in(_tk, 200 + f), (512,), 0, v, jnp.int32) for f, v in enumerate([125000, 12500, 1250, 1000, 1250, 12500, 12500, 1000, 1000, 12500, 1000, 1250, 1250, 1250, 1250, 1250, 1000, 1000, 1250, 12500, 1000, 1000, 1250, 1000, 1250, 1000])], axis=1)
        tbl_0 = 0.05 * jax.random.normal(jax.random.fold_in(_tk, 500 + 0), (125000, 128), jnp.float32)
        tbl_1 = 0.05 * jax.random.normal(jax.random.fold_in(_tk, 500 + 1), (12500, 128), jnp.float32)
        tbl_2 = 0.05 * jax.random.normal(jax.random.fold_in(_tk, 500 + 2), (1250, 128), jnp.float32)
        tbl_3 = 0.05 * jax.random.normal(jax.random.fold_in(_tk, 500 + 3), (1000, 128), jnp.float32)
        tbl_4 = 0.05 * jax.random.normal(jax.random.fold_in(_tk, 500 + 4), (1250, 128), jnp.float32)
        tbl_5 = 0.05 * jax.random.normal(jax.random.fold_in(_tk, 500 + 5), (12500, 128), jnp.float32)
        tbl_6 = 0.05 * jax.random.normal(jax.random.fold_in(_tk, 500 + 6), (12500, 128), jnp.float32)
        tbl_7 = 0.05 * jax.random.normal(jax.random.fold_in(_tk, 500 + 7), (1000, 128), jnp.float32)
        tbl_8 = 0.05 * jax.random.normal(jax.random.fold_in(_tk, 500 + 8), (1000, 128), jnp.float32)
        tbl_9 = 0.05 * jax.random.normal(jax.random.fold_in(_tk, 500 + 9), (12500, 128), jnp.float32)
        tbl_10 = 0.05 * jax.random.normal(jax.random.fold_in(_tk, 500 + 10), (1000, 128), jnp.float32)
        tbl_11 = 0.05 * jax.random.normal(jax.random.fold_in(_tk, 500 + 11), (1250, 128), jnp.float32)
        tbl_12 = 0.05 * jax.random.normal(jax.random.fold_in(_tk, 500 + 12), (1250, 128), jnp.float32)
        tbl_13 = 0.05 * jax.random.normal(jax.random.fold_in(_tk, 500 + 13), (1250, 128), jnp.float32)
        tbl_14 = 0.05 * jax.random.normal(jax.random.fold_in(_tk, 500 + 14), (1250, 128), jnp.float32)
        tbl_15 = 0.05 * jax.random.normal(jax.random.fold_in(_tk, 500 + 15), (1250, 128), jnp.float32)
        tbl_16 = 0.05 * jax.random.normal(jax.random.fold_in(_tk, 500 + 16), (1000, 128), jnp.float32)
        tbl_17 = 0.05 * jax.random.normal(jax.random.fold_in(_tk, 500 + 17), (1000, 128), jnp.float32)
        tbl_18 = 0.05 * jax.random.normal(jax.random.fold_in(_tk, 500 + 18), (1250, 128), jnp.float32)
        tbl_19 = 0.05 * jax.random.normal(jax.random.fold_in(_tk, 500 + 19), (12500, 128), jnp.float32)
        tbl_20 = 0.05 * jax.random.normal(jax.random.fold_in(_tk, 500 + 20), (1000, 128), jnp.float32)
        tbl_21 = 0.05 * jax.random.normal(jax.random.fold_in(_tk, 500 + 21), (1000, 128), jnp.float32)
        tbl_22 = 0.05 * jax.random.normal(jax.random.fold_in(_tk, 500 + 22), (1250, 128), jnp.float32)
        tbl_23 = 0.05 * jax.random.normal(jax.random.fold_in(_tk, 500 + 23), (1000, 128), jnp.float32)
        tbl_24 = 0.05 * jax.random.normal(jax.random.fold_in(_tk, 500 + 24), (1250, 128), jnp.float32)
        tbl_25 = 0.05 * jax.random.normal(jax.random.fold_in(_tk, 500 + 25), (1000, 128), jnp.float32)
        _rk = jax.random.fold_in(_tk, 7)
        r_dense_features = -0.000520686 + 1.00062 * jax.random.normal(jax.random.fold_in(_rk, 101), (512, 128), jnp.float32)
        W_top1 = 0.0405887 * jax.random.normal(jax.random.fold_in(_tk, 801), (607, 512), jnp.float32)
        W_top2 = 0.0441942 * jax.random.normal(jax.random.fold_in(_tk, 802), (512, 256), jnp.float32)
        W_top3 = 0.0625 * jax.random.normal(jax.random.fold_in(_tk, 803), (256, 1), jnp.float32)
        b_top1 = jnp.zeros((512,), jnp.float32)
        b_top2 = jnp.zeros((256,), jnp.float32)
        return (r_dense_features, ids, tbl_0, tbl_1, tbl_2, tbl_3, tbl_4, tbl_5, tbl_6, tbl_7, tbl_8, tbl_9, tbl_10, tbl_11, tbl_12, tbl_13, tbl_14, tbl_15, tbl_16, tbl_17, tbl_18, tbl_19, tbl_20, tbl_21, tbl_22, tbl_23, tbl_24, tbl_25, W_top1, b_top1, W_top2, b_top2, W_top3)
    r_dense_features, ids, tbl_0, tbl_1, tbl_2, tbl_3, tbl_4, tbl_5, tbl_6, tbl_7, tbl_8, tbl_9, tbl_10, tbl_11, tbl_12, tbl_13, tbl_14, tbl_15, tbl_16, tbl_17, tbl_18, tbl_19, tbl_20, tbl_21, tbl_22, tbl_23, tbl_24, tbl_25, W_top1, b_top1, W_top2, b_top2, W_top3 = _rec_inputs()

    def _L0_rec_setup():
        import jax, jax.numpy as jnp
        import numpy as np
        F = 26
        N = F + 1
        _TRIU_I, _TRIU_J = np.triu_indices(N, k=1)
        key = jax.random.key(seed)
        k1, k2 = jax.random.split(key)
        B, D = (2048, 128)
        dense_features = jax.random.normal(k1, (B, D), dtype=jnp.float32)
        sparse_features = jax.random.normal(k2, (B, F, D), dtype=jnp.float32)
        return {'dense_features': dense_features, 'sparse_features': sparse_features}
    _L0_rec_all = _L0_rec_setup()
    _L0_rec_in = {k: v for k, v in _L0_rec_all.items() if k in ()}
    del _L0_rec_all
    return {'r_dense_features': r_dense_features, 'ids': ids, 'tbl_0': tbl_0, 'tbl_1': tbl_1, 'tbl_2': tbl_2, 'tbl_3': tbl_3, 'tbl_4': tbl_4, 'tbl_5': tbl_5, 'tbl_6': tbl_6, 'tbl_7': tbl_7, 'tbl_8': tbl_8, 'tbl_9': tbl_9, 'tbl_10': tbl_10, 'tbl_11': tbl_11, 'tbl_12': tbl_12, 'tbl_13': tbl_13, 'tbl_14': tbl_14, 'tbl_15': tbl_15, 'tbl_16': tbl_16, 'tbl_17': tbl_17, 'tbl_18': tbl_18, 'tbl_19': tbl_19, 'tbl_20': tbl_20, 'tbl_21': tbl_21, 'tbl_22': tbl_22, 'tbl_23': tbl_23, 'tbl_24': tbl_24, 'tbl_25': tbl_25, 'W_top1': W_top1, 'b_top1': b_top1, 'W_top2': W_top2, 'b_top2': b_top2, 'W_top3': W_top3}

def reference(r_dense_features, ids, tbl_0, tbl_1, tbl_2, tbl_3, tbl_4, tbl_5, tbl_6, tbl_7, tbl_8, tbl_9, tbl_10, tbl_11, tbl_12, tbl_13, tbl_14, tbl_15, tbl_16, tbl_17, tbl_18, tbl_19, tbl_20, tbl_21, tbl_22, tbl_23, tbl_24, tbl_25, W_top1, b_top1, W_top2, b_top2, W_top3):
    import jax
    import jax.numpy as jnp

    def _L0_rec_ref(dense_features, sparse_features):
        import jax, jax.numpy as jnp
        import numpy as np
        F = 26
        N = F + 1
        _TRIU_I, _TRIU_J = np.triu_indices(N, k=1)
        combined = jnp.concatenate([dense_features[:, None, :], sparse_features], axis=1)
        interactions = jnp.einsum('bnd,bmd->bnm', combined, combined)
        interactions_flat = interactions[:, _TRIU_I, _TRIU_J]
        return jnp.concatenate([dense_features, interactions_flat], axis=1)
    e = jnp.stack([tbl_0[ids[:, 0]], tbl_1[ids[:, 1]], tbl_2[ids[:, 2]], tbl_3[ids[:, 3]], tbl_4[ids[:, 4]], tbl_5[ids[:, 5]], tbl_6[ids[:, 6]], tbl_7[ids[:, 7]], tbl_8[ids[:, 8]], tbl_9[ids[:, 9]], tbl_10[ids[:, 10]], tbl_11[ids[:, 11]], tbl_12[ids[:, 12]], tbl_13[ids[:, 13]], tbl_14[ids[:, 14]], tbl_15[ids[:, 15]], tbl_16[ids[:, 16]], tbl_17[ids[:, 17]], tbl_18[ids[:, 18]], tbl_19[ids[:, 19]], tbl_20[ids[:, 20]], tbl_21[ids[:, 21]], tbl_22[ids[:, 22]], tbl_23[ids[:, 23]], tbl_24[ids[:, 24]], tbl_25[ids[:, 25]]], axis=1)
    z = _L0_rec_ref(r_dense_features, e)
    z = z.reshape(z.shape[0], -1)
    h = jnp.concatenate([z, r_dense_features], axis=1)
    h = jnp.maximum(h @ W_top1 + b_top1, 0.0)
    h = jnp.maximum(h @ W_top2 + b_top2, 0.0)
    y = h @ W_top3
    return y

_drawn_inputs = setup_inputs


def setup_inputs(seed=0):
    import zlib

    import numpy as np

    out = dict(_drawn_inputs(seed))
    spreads = {'b_top1': (0.0, 0.1), 'b_top2': (0.0, 0.1)}
    factors = {}
    for name, (base, spread) in spreads.items():
        noise = np.random.default_rng([zlib.crc32(name.encode()), seed]).standard_normal(out[name].shape)
        drawn = base * np.exp(spread * noise) if base else spread * noise
        out[name] = jnp.asarray(drawn.astype(out[name].dtype))
    for name, factor in factors.items():
        out[name] = (out[name] * factor).astype(out[name].dtype)
    return out
```

```python
import concourse.bass as bass
from concourse import mybir
from contextlib import ExitStack

B = 512
NF = 26
NS = NF + 1
D = 128
P = 128
NT = B // P
SP_ = 32
NPAIR = NS * (NS - 1) // 2
NC = 3
PC = NPAIR // NC
H1, H2 = 512, 256
K1, K2 = H1 // P, H2 // P
GS = 4
NG = -(-NS // GS)
SB = 4
GB = 4
NQ = P // (SB * GB)


def group_slots(g):
    return range(g * GS, min(g * GS + GS, NS))


def first_pair(j):
    return j * (j - 1) // 2


def pair_rows():
    return [i * NS - i * (i + 1) // 2 + j - i - 1 for j in range(1, NS) for i in range(j)]


def dlrm_tower(nc, dense, ids, tables, w1_dense, w1_pairs, b1, w2, b2, w3, out):
    fp32 = mybir.dt.float32
    ALU = mybir.AluOpType
    ACT = mybir.ActivationFunctionType

    with ExitStack() as ctx:
        def sb(name, shape, dt=fp32):
            return ctx.enter_context(nc.sbuf_tensor(name, shape, dt))

        def bank(name):
            return ctx.enter_context(nc.psum_tensor(name, [P, 512], fp32))

        def sem(name):
            return ctx.enter_context(nc.semaphore(name))

        index = sb("index", [P, NT, NF], mybir.dt.int32)
        rows = sb("rows", [P, NT, NS, D])
        cols = sb("cols", [P, B, SP_])
        gram = sb("gram", [NS, NS, P])
        flat = sb("flat", [P, NPAIR])
        pairs = sb("pairs", [PC, NC, P])
        w1d = sb("w1d", [P, 2, H1])
        w1s = sb("w1s", [P, H1])
        w1p = sb("w1p", [PC, NC, H1])
        w2s = sb("w2s", [P, K1, H2])
        w3s = sb("w3s", [P, K2])
        b1s = sb("b1s", [P, K1])
        b2s = sb("b2s", [P, K2])
        h1 = sb("h1", [P, K1, P])
        h2 = sb("h2", [P, K2, P])
        y = sb("y", [1, B])
        ident = sb("ident", [P, P])

        turn_ps = [bank("turn_ps0"), bank("turn_ps1")]
        gram_ps = [bank("gram_ps0"), bank("gram_ps1")]
        flat_ps = bank("flat_ps")
        pair_ps = bank("pair_ps")
        h1_ps = bank("h1_ps")
        h2_ps = bank("h2_ps")

        ids_loaded = sem("ids_loaded")
        dense_loaded = sem("dense_loaded")
        w1d_loaded = sem("w1d_loaded")
        weights_loaded = sem("weights_loaded")
        gathered = [[sem(f"gathered{t}_{g}") for g in range(NG)] for t in range(NT)]
        ident_zeroed = sem("ident_zeroed")
        ident_ready = sem("ident_ready")
        pad_zeroed = sem("pad_zeroed")
        w1_summed = sem("w1_summed")
        turned = sem("turned")
        stored = [sem("stored_v"), sem("stored_a")]
        multiplied = sem("multiplied")
        picked = [sem("picked_v"), sem("picked_a")]
        flat_turned = sem("flat_turned")
        flat_stored = sem("flat_stored")
        pairs_turned = sem("pairs_turned")
        pairs_stored = sem("pairs_stored")
        h1_summed = sem("h1_summed")
        h1_stored = sem("h1_stored")
        h2_summed = sem("h2_summed")
        h2_stored = sem("h2_stored")
        y_summed = sem("y_summed")
        y_stored = sem("y_stored")
        out_written = sem("out_written")

        block = ctx.enter_context(nc.Block())

        def groups_before(n, who):
            return (n + 1 - who) // 2

        def store_group(eng, copy, t, g):
            n = t * NG + g
            slots = group_slots(g)
            k = len(slots)
            eng.wait_ge(turned, n + 1)
            copy(cols[:, t * P:(t + 1) * P, slots[0]:slots[0] + k],
                 turn_ps[n % 2][:, 0:k * P].rearrange("p (s b) -> p b s", s=k)).then_inc(stored[n % 2], 1)

        def pick_blocks(eng, copy, t, q, who):
            m = t * NQ + q
            eng.wait_ge(multiplied, m + 1)
            for s in (2 * who, 2 * who + 1):
                src = gram_ps[m % 2][SP_ * s:SP_ * s + NS, 0:GB * SB * NS] \
                    .rearrange("p (k s j) -> p k s j", k=GB, s=SB)[:, :, s, :]
                first = q * GB * SB + s
                dst = gram[:, :, first:first + SB * (GB - 1) + 1:SB].rearrange("p j k -> p k j")
                last = copy(dst, src)
            last.then_inc(picked[who], 1)

        @block.sync
        def _(sp):
            sp.dma_start(index[:], ids.rearrange("(t p) f -> p t f", p=P)).then_inc(ids_loaded, 16)
            sp.dma_start(rows[:, :, 0, :], dense.rearrange("(t p) d -> p t d", p=P)).then_inc(dense_loaded, 16)
            sp.dma_start(w1d[:], w1_dense.rearrange("(a p) o -> p a o", p=P)).then_inc(w1d_loaded, 16)
            sp.dma_start(w1p[:], w1_pairs.rearrange("(c p) o -> p c o", p=PC)).then_inc(weights_loaded, 16)
            sp.dma_start(w2s[:], w2.rearrange("(k p) o -> p k o", p=P)).then_inc(weights_loaded, 16)
            sp.dma_start(w3s[:], w3).then_inc(weights_loaded, 16)
            sp.dma_start(b1s[:], b1).then_inc(weights_loaded, 16)
            sp.dma_start(b2s[:], b2).then_inc(weights_loaded, 16)
            sp.wait_ge(y_stored, NT)
            sp.dma_start(out.rearrange("b a -> a b"), y[:]).then_inc(out_written, 16)
            sp.wait_ge(out_written, 16)

        @block.gpsimd
        def _(pool):
            pool.memset(ident[:], 0.0).then_inc(ident_zeroed, 1)
            pool.wait_ge(ident_zeroed, 1)
            pool.affine_select(out=ident[:], in_=ident[:], compare_op=ALU.not_equal, fill=1.0, base=0,
                               pattern=[[-1, P]], channel_multiplier=1).then_inc(ident_ready, 1)
            pool.wait_ge(ids_loaded, 16)
            for t in range(NT):
                for f in range(NF):
                    pool.indirect_dma_start(rows[:, t, f + 1, :], None, tables[f],
                                            bass.IndirectOffsetOnAxis(index[:, t, f:f + 1], 0)) \
                        .then_inc(gathered[t][(f + 1) // GS], 16)

        @block.vector
        def _(dve):
            nc.vector.memset(cols[:, :, NS:SP_], 0.0).then_inc(pad_zeroed, 1)
            dve.wait_ge(w1d_loaded, 16)
            nc.vector.tensor_add(w1s[:], w1d[:, 0, :], w1d[:, 1, :]).then_inc(w1_summed, 1)
            for t in range(NT):
                for g in range(NG):
                    if (t * NG + g) % 2 == 0:
                        store_group(dve, nc.vector.tensor_copy, t, g)
                for q in range(NQ):
                    pick_blocks(dve, nc.vector.tensor_copy, t, q, 0)
                dve.wait_ge(flat_turned, t + 1)
                nc.vector.tensor_copy(flat[:], flat_ps[:, 0:NPAIR]).then_inc(flat_stored, 1)
                dve.wait_ge(pairs_turned, t + 1)
                nc.vector.tensor_copy(pairs[:], pair_ps[0:PC, 0:NC * P].rearrange("p (c b) -> p c b", c=NC)) \
                    .then_inc(pairs_stored, 1)

        @block.scalar
        def _(act):
            for t in range(NT):
                for g in range(NG):
                    if (t * NG + g) % 2 == 1:
                        store_group(act, nc.scalar.copy, t, g)
                for q in range(NQ):
                    pick_blocks(act, nc.scalar.copy, t, q, 1)
                act.wait_ge(h1_summed, t + 1)
                act.wait_ge(weights_loaded, 5 * 16)
                for k in range(K1):
                    last = nc.scalar.activation(h1[:, k, :], h1_ps[:, k * P:(k + 1) * P], ACT.Relu,
                                                bias=b1s[:, k:k + 1])
                last.then_inc(h1_stored, 1)
                act.wait_ge(h2_summed, t + 1)
                for k in range(K2):
                    last = nc.scalar.activation(h2[:, k, :], h2_ps[:, k * P:(k + 1) * P], ACT.Relu,
                                                bias=b2s[:, k:k + 1])
                last.then_inc(h2_stored, 1)
                act.wait_ge(y_summed, t + 1)
                nc.scalar.copy(y[0:1, t * P:(t + 1) * P], h2_ps[0:1, K2 * P:(K2 + 1) * P]).then_inc(y_stored, 1)

        @block.tensor
        def _(pe):
            pe.wait_ge(ident_ready, 1)
            for t in range(NT):
                for g in range(NG):
                    n = t * NG + g
                    slots = group_slots(g)
                    if g == 0 and t == 0:
                        pe.wait_ge(dense_loaded, 16)
                    pe.wait_ge(gathered[t][g], 16 * sum(s > 0 for s in slots))
                    if n >= 2:
                        pe.wait_ge(stored[n % 2], groups_before(n, n % 2))
                    for k, s in enumerate(slots):
                        last = nc.tensor.transpose(turn_ps[n % 2][:, k * P:(k + 1) * P], rows[:, t, s, :], ident[:])
                    last.then_inc(turned, 1)
                if t == 0:
                    pe.wait_ge(pad_zeroed, 1)
                for who in range(2):
                    pe.wait_ge(stored[who], groups_before((t + 1) * NG, who))
                for q in range(NQ):
                    m = t * NQ + q
                    if m >= 2:
                        pe.wait_ge(picked[0], m - 1)
                        pe.wait_ge(picked[1], m - 1)
                    for k in range(GB):
                        b = t * P + (q * GB + k) * SB
                        last = nc.tensor.matmul(gram_ps[m % 2][:, k * SB * NS:(k + 1) * SB * NS],
                                                cols[:, b:b + SB, :], cols[:, b:b + SB, 0:NS], start=True, stop=True)
                    last.then_inc(multiplied, 1)
                pe.wait_ge(picked[0], (t + 1) * NQ)
                pe.wait_ge(picked[1], (t + 1) * NQ)
                if t >= 1:
                    pe.wait_ge(flat_stored, t)
                for j in range(1, NS):
                    last = nc.tensor.transpose(flat_ps[:, first_pair(j):first_pair(j) + j], gram[0:j, j, :],
                                               ident[0:j, 0:j])
                last.then_inc(flat_turned, 1)
                pe.wait_ge(flat_stored, t + 1)
                if t >= 1:
                    pe.wait_ge(pairs_stored, t)
                for c in range(NC):
                    last = nc.tensor.transpose(pair_ps[0:PC, c * P:(c + 1) * P], flat[:, c * PC:(c + 1) * PC], ident[:])
                last.then_inc(pairs_turned, 1)
                if t == 0:
                    pe.wait_ge(w1_summed, 1)
                    pe.wait_ge(weights_loaded, 5 * 16)
                pe.wait_ge(pairs_stored, t + 1)
                if t >= 1:
                    pe.wait_ge(h1_stored, t)
                for k in range(K1):
                    o = slice(k * P, (k + 1) * P)
                    nc.tensor.matmul(h1_ps[:, o], w1s[:, o], cols[:, t * P:(t + 1) * P, 0], start=True, stop=False)
                    for c in range(NC):
                        last = nc.tensor.matmul(h1_ps[:, o], w1p[:, c, o], pairs[:, c, :], start=False, stop=c == NC - 1)
                last.then_inc(h1_summed, 1)
                pe.wait_ge(h1_stored, t + 1)
                if t >= 1:
                    pe.wait_ge(y_stored, t)
                for m in range(K2):
                    for k in range(K1):
                        last = nc.tensor.matmul(h2_ps[:, m * P:(m + 1) * P], w2s[:, k, m * P:(m + 1) * P], h1[:, k, :],
                                                start=k == 0, stop=k == K1 - 1)
                last.then_inc(h2_summed, 1)
                pe.wait_ge(h2_stored, t + 1)
                for k in range(K2):
                    last = nc.tensor.matmul(h2_ps[0:1, K2 * P:(K2 + 1) * P], w3s[:, k:k + 1], h2[:, k, :],
                                            start=k == 0, stop=k == K2 - 1)
                last.then_inc(y_summed, 1)


def kernel(**inputs):
    import numpy as np
    import concourse.bacc as bacc
    from concourse.bass_utils import run_bass_kernel_spmd as run

    nc = bacc.Bacc("TRN2", target_bir_lowering=False, num_devices=1)
    arrays = {}

    def given(name, a):
        arrays[name] = np.ascontiguousarray(a)
        return nc.dram_tensor(name, arrays[name].shape, mybir.dt.from_np(arrays[name].dtype),
                              kind="ExternalInput").ap()

    w1 = np.asarray(inputs["W_top1"])
    pair_at = D + np.array(pair_rows())
    args = [
        given("dense", inputs["r_dense_features"]),
        given("ids", inputs["ids"]),
        [given(f"tbl_{f}", inputs[f"tbl_{f}"]) for f in range(NF)],
        given("w1_dense", np.concatenate([w1[:D], w1[D + NPAIR:]])),
        given("w1_pairs", w1[pair_at]),
        given("b1", np.asarray(inputs["b_top1"]).reshape(K1, P).T),
        given("w2", inputs["W_top2"]),
        given("b2", np.asarray(inputs["b_top2"]).reshape(K2, P).T),
        given("w3", np.asarray(inputs["W_top3"]).reshape(K2, P).T),
    ]
    out = nc.dram_tensor("out", (B, 1), mybir.dt.float32, kind="ExternalOutput").ap()
    dlrm_tower(nc, *args, out)
    result = run(nc, [arrays], core_ids=[0])
    return result.results[0]["out"]
```

```python
import concourse.bass as bass
from concourse import mybir
from contextlib import ExitStack

B = 512
NF = 26
NS = NF + 1
D = 128
P = 128
NT = B // P
SP_ = 32
NPAIR = NS * (NS - 1) // 2
NC = 3
PC = NPAIR // NC
H1, H2 = 512, 256
K1, K2 = H1 // P, H2 // P
GS = 4
SB = 4
GB = 4
NQ = P // (SB * GB)
ROWS = [125000, 12500, 1250, 1000, 1250, 12500, 12500, 1000, 1000, 12500, 1000, 1250, 1250, 1250, 1250, 1250, 1000,
        1000, 1250, 12500, 1000, 1000, 1250, 1000, 1250, 1000]
HOT_ROWS = 1000
HC = 8
HP = HOT_ROWS // HC
HP16 = HP // 16 * 16
HOT = [f for f in range(NF) if ROWS[f] == HOT_ROWS][-6:]
COLD = [f for f in range(NF) if f not in HOT]
NH = len(HOT)
HV = 7
NR = 1 + len(COLD)
SLOTS = [0] + [f + 1 for f in COLD] + [f + 1 for f in HOT]
NG = -(-NR // GS)


def group_slots(g):
    return range(g * GS, min(g * GS + GS, NR))


def first_turns(k):
    return range(k, k + 1 if k < NH - 1 else NG)


def first_pair(j):
    return j * (j - 1) // 2


def pair_rows():
    ordered = [sorted((SLOTS[i], SLOTS[j])) for j in range(1, NS) for i in range(j)]
    return [i * NS - i * (i + 1) // 2 + j - i - 1 for i, j in ordered]


def dlrm_tower(nc, dense, ids, hot_ids, tables, w1_dense, w1_pairs, b1, w2, b2, w3, out):
    fp32 = mybir.dt.float32
    fp32r = mybir.dt.float32r
    ALU = mybir.AluOpType
    ACT = mybir.ActivationFunctionType

    with ExitStack() as ctx:
        def sb(name, shape, dt=fp32):
            return ctx.enter_context(nc.sbuf_tensor(name, shape, dt))

        def bank(name):
            return ctx.enter_context(nc.psum_tensor(name, [P, 512], fp32))

        def sem(name):
            return ctx.enter_context(nc.semaphore(name))

        index = sb("index", [P, NT, NF], mybir.dt.int32)
        rows = sb("rows", [P, NT, NR, D])
        cols = sb("cols", [P, B, SP_])
        gram = sb("gram", [NS, NS, P])
        flat = sb("flat", [P, NPAIR])
        pairs = sb("pairs", [PC, NC, P])
        w1d = sb("w1d", [P, 2, H1])
        w1s = sb("w1s", [P, H1])
        w1p = sb("w1p", [PC, NC, H1])
        w2s = sb("w2s", [P, K1, H2])
        w3s = sb("w3s", [P, K2])
        b1s = sb("b1s", [P, K1])
        b2s = sb("b2s", [P, K2])
        h1 = sb("h1", [P, K1, P])
        h2 = sb("h2", [P, K2, P])
        y = sb("y", [1, B])
        ident = sb("ident", [P, P])
        row_int = sb("row_int", [HP, HC], mybir.dt.int32)
        row_no = sb("row_no", [HP, HC])
        minus_row_no = sb("minus_row_no", [HP, HC])
        distance = sb("distance", [HP, HC - HV, B])
        hot_id = sb("hot_id", [P, 2, B], mybir.dt.int32)
        table = sb("table", [HP, 2, HC * D])
        table_hi = sb("table_hi", [HP, 2, HC * D], fp32r)
        table_lo = sb("table_lo", [HP, 2, HC * D], fp32r)
        hot = sb("hot", [HP, HC, B], fp32r)

        turn_ps = [bank("turn_ps0"), bank("turn_ps1")]
        gram_ps = [bank("gram_ps0"), bank("gram_ps1")]
        flat_ps = bank("flat_ps")
        h1_ps = [bank("h1_ps0"), bank("h1_ps1")]
        h2_ps = bank("h2_ps")

        ids_loaded = sem("ids_loaded")
        dense_loaded = sem("dense_loaded")
        w1d_loaded = sem("w1d_loaded")
        weights_loaded = sem("weights_loaded")
        table_loaded = [sem("table_loaded0"), sem("table_loaded1")]
        gathered = [[sem(f"gathered{t}_{g}") for g in range(NG)] for t in range(NT)]
        ident_zeroed = sem("ident_zeroed")
        ident_ready = sem("ident_ready")
        row_counted = sem("row_counted")
        row_ready = sem("row_ready")
        pad_zeroed = sem("pad_zeroed")
        w1_summed = sem("w1_summed")
        hi_ready = sem("hi_ready")
        lo_ready = sem("lo_ready")
        hot_ready_v = sem("hot_ready_v")
        hot_ready_a = sem("hot_ready_a")
        far = sem("far")
        hot_used = sem("hot_used")
        hot_stored = sem("hot_stored")
        turned = sem("turned")
        stored = sem("stored")
        multiplied = sem("multiplied")
        picked_v = sem("picked_v")
        picked_a = sem("picked_a")
        flat_turned = sem("flat_turned")
        flat_stored = sem("flat_stored")
        pairs_turned = sem("pairs_turned")
        pairs_stored = sem("pairs_stored")
        h1_summed = sem("h1_summed")
        h1_stored_a = sem("h1_stored_a")
        h1_stored_v = sem("h1_stored_v")
        h2_summed = sem("h2_summed")
        h2_stored = sem("h2_stored")
        y_summed = sem("y_summed")
        y_stored = sem("y_stored")
        out_written = sem("out_written")

        block = ctx.enter_context(nc.Block())
        KH = K1 // 2

        def pick_blocks(copy, t, q, quadrants):
            for s in quadrants:
                src = gram_ps[(t * NQ + q) % 2][SP_ * s:SP_ * s + NS, 0:GB * SB * NS] \
                    .rearrange("p (k s j) -> p k s j", k=GB, s=SB)[:, :, s, :]
                first = q * GB * SB + s
                dst = gram[:, :, first:first + SB * (GB - 1) + 1:SB].rearrange("p j k -> p k j")
                last = copy(dst, src)
            return last

        @block.sync
        def _(sp):
            def load_table(k):
                f = HOT[k]
                src = tables[f].rearrange("(p c) d -> p (c d)", c=HC)
                if k >= 2:
                    sp.wait_ge(lo_ready, k - 1)
                    sp.wait_ge(hot_ready_v, (k - 1) * HV)
                    sp.wait_ge(hot_ready_a, (k - 1) * (HC - HV))
                sp.dma_start(hot_id[:, k % 2, :], hot_ids[k:k + 1, :].to_broadcast([P, B])) \
                    .then_inc(table_loaded[k % 2], 16)
                sp.dma_start(table[0:HP16, k % 2, :], src[0:HP16, :]).then_inc(table_loaded[k % 2], 16)
                sp.dma_start(table[HP16:HP, k % 2, :], src[HP16:HP, :]).then_inc(table_loaded[k % 2], 16)

            sp.dma_start(index[:], ids.rearrange("(t p) f -> p t f", p=P)).then_inc(ids_loaded, 16)
            load_table(0)
            load_table(1)
            sp.dma_start(rows[:, :, 0, :], dense.rearrange("(t p) d -> p t d", p=P)).then_inc(dense_loaded, 16)
            sp.dma_start(w1d[:], w1_dense.rearrange("(a p) o -> p a o", p=P)).then_inc(w1d_loaded, 16)
            for k in range(2, NH):
                load_table(k)
            sp.dma_start(w1p[:], w1_pairs.rearrange("(c p) o -> p c o", p=PC)).then_inc(weights_loaded, 16)
            sp.dma_start(w2s[:], w2.rearrange("(k p) o -> p k o", p=P)).then_inc(weights_loaded, 16)
            sp.dma_start(w3s[:], w3).then_inc(weights_loaded, 16)
            sp.dma_start(b1s[:], b1).then_inc(weights_loaded, 16)
            sp.dma_start(b2s[:], b2).then_inc(weights_loaded, 16)
            sp.wait_ge(y_stored, NT)
            sp.dma_start(out.rearrange("b a -> a b"), y[:]).then_inc(out_written, 16)
            sp.wait_ge(out_written, 16)

        @block.gpsimd
        def _(pool):
            pool.iota(row_int[:], pattern=[[1, HC]], base=0, channel_multiplier=HC).then_inc(row_counted, 1)
            pool.memset(ident[:], 0.0).then_inc(ident_zeroed, 1)
            pool.wait_ge(ident_zeroed, 1)
            pool.affine_select(out=ident[:], in_=ident[:], compare_op=ALU.not_equal, fill=1.0, base=0,
                               pattern=[[-1, P]], channel_multiplier=1).then_inc(ident_ready, 1)
            pool.wait_ge(ids_loaded, 16)
            for t in range(NT):
                for n, f in enumerate(COLD):
                    pool.indirect_dma_start(rows[:, t, n + 1, :], None, tables[f],
                                            bass.IndirectOffsetOnAxis(index[:, t, f:f + 1], 0)) \
                        .then_inc(gathered[t][(n + 1) // GS], 16)

        @block.vector
        def _(dve):
            dve.wait_ge(row_counted, 1)
            nc.vector.tensor_copy(row_no[:], row_int[:]).then_inc(row_ready, 1)
            nc.vector.tensor_scalar(minus_row_no[:], row_int[:], -1.0, None, ALU.mult).then_inc(row_ready, 1)
            nc.vector.memset(cols[:, :, NS:SP_], 0.0).then_inc(pad_zeroed, 1)
            dve.wait_ge(row_ready, 1)

            def split_table(k):
                dve.wait_ge(table_loaded[k % 2], 3 * 16 * (k // 2 + 1))
                dve.wait_ge(hi_ready, k + 1)
                if k >= 2:
                    dve.wait_ge(hot_used, (k - 1) * HC)
                nc.vector.tensor_tensor(table_lo[:, k % 2, :], table[:, k % 2, :], table_hi[:, k % 2, :],
                                        ALU.subtract).then_inc(lo_ready, 1)

            for k in range(NH):
                dve.wait_ge(table_loaded[k % 2], 3 * 16 * (k // 2 + 1))
                for c in range(HV):
                    if k >= 1:
                        dve.wait_ge(hot_used, (k - 1) * HC + c + 1)
                    nc.vector.tensor_scalar(hot[:, c, :], hot_id[0:HP, k % 2, :], row_no[:, c:c + 1], None,
                                            ALU.is_equal).then_inc(hot_ready_v, 1)
                    if k == 0 and c == HV // 2:
                        split_table(0)
                if k + 1 < NH:
                    split_table(k + 1)
            dve.wait_ge(w1d_loaded, 16)
            nc.vector.tensor_add(w1s[:], w1d[:, 0, :], w1d[:, 1, :]).then_inc(w1_summed, 1)
            dve.wait_ge(weights_loaded, 5 * 16)
            for t in range(NT):
                for q in range(NQ):
                    dve.wait_ge(multiplied, t * NQ + q + 1)
                    pick_blocks(nc.vector.tensor_copy, t, q, (0, 1)).then_inc(picked_v, 1)
                dve.wait_ge(flat_turned, t + 1)
                nc.vector.tensor_copy(flat[:], flat_ps[:, 0:NPAIR]).then_inc(flat_stored, 1)
                dve.wait_ge(pairs_turned, t + 1)
                for c in range(NC):
                    nc.vector.tensor_copy(pairs[:, c, :], flat_ps[0:PC, c * P:(c + 1) * P]).then_inc(pairs_stored, 1)
                dve.wait_ge(h1_summed, 2 * t + 2)
                for k in range(KH, K1):
                    last = nc.vector.tensor_scalar(h1[:, k, :], h1_ps[1][:, (k - KH) * P:(k - KH + 1) * P],
                                                   b1s[:, k:k + 1], 0.0, ALU.add, ALU.max)
                last.then_inc(h1_stored_v, 1)

        @block.scalar
        def _(act):
            def store_group(t, g):
                n = t * NG + g
                slots = group_slots(g)
                k = len(slots)
                act.wait_ge(turned, n + 1)
                nc.scalar.copy(cols[:, t * P:(t + 1) * P, slots[0]:slots[0] + k],
                               turn_ps[n % 2][:, 0:k * P].rearrange("p (s b) -> p b s", s=k)).then_inc(stored, 1)

            def store_hot(k):
                act.wait_ge(hot_used, (k + 1) * HC)
                nc.scalar.copy(cols[:, :, NR + k], h1_ps[k % 2][:]).then_inc(hot_stored, 1)

            def round_table(k):
                act.wait_ge(table_loaded[k % 2], 3 * 16 * (k // 2 + 1))
                if k >= 2:
                    act.wait_ge(hot_used, (k - 1) * HC)
                nc.scalar.copy(table_hi[:, k % 2, :], table[:, k % 2, :]).then_inc(hi_ready, 1)

            def store_h1(t):
                act.wait_ge(h1_summed, 2 * t + 1)
                if t == 0:
                    act.wait_ge(weights_loaded, 5 * 16)
                for k in range(KH):
                    last = nc.scalar.activation(h1[:, k, :], h1_ps[0][:, k * P:(k + 1) * P], ACT.Relu,
                                                bias=b1s[:, k:k + 1])
                last.then_inc(h1_stored_a, 1)

            def store_h2(t):
                act.wait_ge(h2_summed, t + 1)
                for k in range(K2):
                    last = nc.scalar.activation(h2[:, k, :], h2_ps[:, k * P:(k + 1) * P], ACT.Relu,
                                                bias=b2s[:, k:k + 1])
                last.then_inc(h2_stored, 1)

            def store_y(t):
                act.wait_ge(y_summed, t + 1)
                nc.scalar.copy(y[0:1, t * P:(t + 1) * P], h2_ps[0:1, K2 * P:(K2 + 1) * P]).then_inc(y_stored, 1)

            def make_hot(k):
                for c in range(HV, HC):
                    if k >= 1:
                        act.wait_ge(hot_ready_a, k * (HC - HV))
                    nc.scalar.activation(distance[:, c - HV, :], hot_id[0:HP, k % 2, :], ACT.Abs,
                                         bias=minus_row_no[:, c:c + 1]).then_inc(far, 1)
                for c in range(HV, HC):
                    act.wait_ge(far, k * (HC - HV) + c - HV + 1)
                    if k >= 1:
                        act.wait_ge(hot_used, (k - 1) * HC + c + 1)
                    nc.scalar.activation(hot[:, c, :], distance[:, c - HV, :], ACT.Relu, bias=1.0, scale=-1.0) \
                        .then_inc(hot_ready_a, 1)

            round_table(0)
            act.wait_ge(row_ready, 2)
            for k in range(NH):
                make_hot(k)
                if k + 1 < NH:
                    round_table(k + 1)
                store_hot(k)
                for g in first_turns(k):
                    store_group(0, g)
            for t in range(NT + 1):
                if t >= 1:
                    if t < NT:
                        store_group(t, 0)
                        store_group(t, 1)
                    store_h1(t - 1)
                    if t < NT:
                        store_group(t, 2)
                    store_h2(t - 1)
                    if t < NT:
                        for g in range(3, NG):
                            store_group(t, g)
                    store_y(t - 1)
                if t < NT:
                    for q in range(NQ):
                        act.wait_ge(multiplied, t * NQ + q + 1)
                        pick_blocks(nc.scalar.copy, t, q, (2, 3)).then_inc(picked_a, 1)

        @block.tensor
        def _(pe):
            def look_up(k):
                if k >= 2:
                    pe.wait_ge(hot_stored, k - 1)
                pe.wait_ge(hi_ready, k + 1)
                order = [(c, part) for part in range(2) for c in range(HC)] if k == 0 else \
                    [(c, part) for c in range(HC) for part in range(2)]
                for n, (c, part) in enumerate(order):
                    if part == 0 and c < HV:
                        pe.wait_ge(hot_ready_v, k * HV + c + 1)
                    elif part == 0:
                        pe.wait_ge(hot_ready_a, k * (HC - HV) + c - HV + 1)
                    elif c == 0:
                        pe.wait_ge(lo_ready, k + 1)
                    last = nc.tensor.matmul(h1_ps[k % 2][:], (table_hi, table_lo)[part][:, k % 2, c * D:(c + 1) * D],
                                            hot[:, c, :], start=n == 0, stop=n == 2 * HC - 1)
                    if part == 1:
                        last.then_inc(hot_used, 1)

            def turn_group(t, g):
                n = t * NG + g
                slots = group_slots(g)
                if n == 0:
                    pe.wait_ge(dense_loaded, 16)
                pe.wait_ge(gathered[t][g], 16 * sum(s > 0 for s in slots))
                if n >= 2:
                    pe.wait_ge(stored, n - 1)
                for k, s in enumerate(slots):
                    last = nc.tensor.transpose(turn_ps[n % 2][:, k * P:(k + 1) * P], rows[:, t, s, :], ident[:])
                last.then_inc(turned, 1)

            def multiply(t):
                pe.wait_ge(stored, (t + 1) * NG)
                if t == 0:
                    pe.wait_ge(hot_stored, NH)
                    pe.wait_ge(pad_zeroed, 1)
                for q in range(NQ):
                    m = t * NQ + q
                    if m >= 2:
                        pe.wait_ge(picked_v, m - 1)
                        pe.wait_ge(picked_a, m - 1)
                    for k in range(GB):
                        b = t * P + (q * GB + k) * SB
                        last = nc.tensor.matmul(gram_ps[m % 2][:, k * SB * NS:(k + 1) * SB * NS],
                                                cols[:, b:b + SB, :], cols[:, b:b + SB, 0:NS], start=True, stop=True)
                    last.then_inc(multiplied, 1)

            def flatten(t):
                pe.wait_ge(picked_v, (t + 1) * NQ)
                pe.wait_ge(picked_a, (t + 1) * NQ)
                if t >= 1:
                    pe.wait_ge(pairs_stored, NC * t)
                for j in range(1, NS):
                    last = nc.tensor.transpose(flat_ps[:, first_pair(j):first_pair(j) + j], gram[0:j, j, :],
                                               ident[0:j, 0:j])
                last.then_inc(flat_turned, 1)

            def turn_pairs(t):
                pe.wait_ge(flat_stored, t + 1)
                for c in range(NC):
                    last = nc.tensor.transpose(flat_ps[0:PC, c * P:(c + 1) * P], flat[:, c * PC:(c + 1) * PC], ident[:])
                last.then_inc(pairs_turned, 1)

            def h1_sums(k):
                return h1_ps[k // KH][:, k % KH * P:(k % KH + 1) * P]

            def layer_1_dense(t, half):
                if t == 0:
                    pe.wait_ge(w1_summed, 1)
                    pe.wait_ge(hot_stored, NH)
                else:
                    pe.wait_ge((h1_stored_a, h1_stored_v)[half], t)
                for k in range(KH * half, KH * half + KH):
                    nc.tensor.matmul(h1_sums(k), w1s[:, k * P:(k + 1) * P], cols[:, t * P:(t + 1) * P, 0],
                                     start=k % KH == 0, stop=False, skip_group_check=True)

            def layer_1(t):
                if t == 0:
                    pe.wait_ge(weights_loaded, 5 * 16)
                for c in range(NC):
                    pe.wait_ge(pairs_stored, NC * t + c + 1)
                    for k in range(K1):
                        last = nc.tensor.matmul(h1_sums(k), w1p[:, c, k * P:(k + 1) * P], pairs[:, c, :],
                                                start=False, stop=c == NC - 1, skip_group_check=True)
                        if c == NC - 1 and k % KH == KH - 1:
                            last.then_inc(h1_summed, 1)

            def layer_2(t):
                pe.wait_ge(h1_stored_a, t + 1)
                if t >= 1:
                    pe.wait_ge(y_stored, t)
                for k in range(K1):
                    if k == KH:
                        pe.wait_ge(h1_stored_v, t + 1)
                    for m in range(K2):
                        last = nc.tensor.matmul(h2_ps[:, m * P:(m + 1) * P], w2s[:, k, m * P:(m + 1) * P], h1[:, k, :],
                                                start=k == 0 and m == 0, stop=k == K1 - 1, skip_group_check=True)
                last.then_inc(h2_summed, 1)

            def layer_3(t):
                pe.wait_ge(h2_stored, t + 1)
                for k in range(K2):
                    last = nc.tensor.matmul(h2_ps[0:1, K2 * P:(K2 + 1) * P], w3s[:, k:k + 1], h2[:, k, :],
                                            start=k == 0, stop=k == K2 - 1)
                last.then_inc(y_summed, 1)

            for k in range(NH):
                look_up(k)
                if k == 0:
                    pe.wait_ge(ident_ready, 1)
                for g in first_turns(k):
                    turn_group(0, g)
            for t in range(NT + 1):
                if t >= 1:
                    if t < NT:
                        turn_group(t, 0)
                    layer_1_dense(t - 1, 0)
                    flatten(t - 1)
                    layer_1_dense(t - 1, 1)
                    turn_pairs(t - 1)
                    if t < NT:
                        turn_group(t, 1)
                    layer_1(t - 1)
                    if t < NT:
                        turn_group(t, 2)
                    layer_2(t - 1)
                    if t < NT:
                        for g in range(3, NG):
                            turn_group(t, g)
                    layer_3(t - 1)
                if t < NT:
                    multiply(t)


def kernel(**inputs):
    import numpy as np
    import concourse.bacc as bacc
    from concourse.bass_utils import run_bass_kernel_spmd as run

    nc = bacc.Bacc("TRN2", target_bir_lowering=False, num_devices=1)
    arrays = {}

    def given(name, a):
        arrays[name] = np.ascontiguousarray(a)
        return nc.dram_tensor(name, arrays[name].shape, mybir.dt.from_np(arrays[name].dtype),
                              kind="ExternalInput").ap()

    w1 = np.asarray(inputs["W_top1"])
    pair_at = D + np.array(pair_rows())
    args = [
        given("dense", inputs["r_dense_features"]),
        given("ids", inputs["ids"]),
        given("hot_ids", np.asarray(inputs["ids"])[:, HOT].T),
        [given(f"tbl_{f}", inputs[f"tbl_{f}"]) for f in range(NF)],
        given("w1_dense", np.concatenate([w1[:D], w1[D + NPAIR:]])),
        given("w1_pairs", w1[pair_at]),
        given("b1", np.asarray(inputs["b_top1"]).reshape(K1, P).T),
        given("w2", inputs["W_top2"]),
        given("b2", np.asarray(inputs["b_top2"]).reshape(K2, P).T),
        given("w3", np.asarray(inputs["W_top3"]).reshape(K2, P).T),
    ]
    out = nc.dram_tensor("out", (B, 1), mybir.dt.float32, kind="ExternalOutput").ap()
    dlrm_tower(nc, *args, out)
    result = run(nc, [arrays], core_ids=[0])
    return result.results[0]["out"]
```

```python
import concourse.bass as bass
from concourse import mybir
from contextlib import ExitStack

B = 512
NF = 26
NS = NF + 1
D = 128
P = 128
NT = B // P
SP_ = 32
NPAIR = NS * (NS - 1) // 2
NC = 3
PC = NPAIR // NC
JA = 20
H1, H2 = 512, 256
K1, K2 = H1 // P, H2 // P
GS = 4
SB = 4
GB = 4
NQ = P // (SB * GB)
ROWS = [125000, 12500, 1250, 1000, 1250, 12500, 12500, 1000, 1000, 12500, 1000, 1250, 1250, 1250, 1250, 1250, 1000,
        1000, 1250, 12500, 1000, 1000, 1250, 1000, 1250, 1000]
HOT_ROWS = 1000
HC = 8
HP = HOT_ROWS // HC
HP16 = HP // 16 * 16
HOT = [f for f in range(NF) if ROWS[f] == HOT_ROWS][-7:]
COLD = [f for f in range(NF) if f not in HOT]
NH = len(HOT)
NL = 3
HV = 7
NR = 1 + len(COLD)
SLOTS = [0] + [f + 1 for f in COLD] + [f + 1 for f in HOT]
NG = -(-NR // GS)


def group_slots(g):
    return range(g * GS, min(g * GS + GS, NR))


def first_turns(k):
    return range(min(k, NG), min(k + 1, NG) if k < NH - 1 else NG)


def first_pair(j):
    return j * (j - 1) // 2


def pair_rows():
    ordered = [sorted((SLOTS[i], SLOTS[j])) for j in range(1, NS) for i in range(j)]
    return [i * NS - i * (i + 1) // 2 + j - i - 1 for i, j in ordered]


def dlrm_tower(nc, dense, ids, hot_ids, tables, w1_dense, w1_pairs, b1, w2, b2, w3, out):
    fp32 = mybir.dt.float32
    fp32r = mybir.dt.float32r
    ALU = mybir.AluOpType
    ACT = mybir.ActivationFunctionType

    with ExitStack() as ctx:
        def sb(name, shape, dt=fp32):
            return ctx.enter_context(nc.sbuf_tensor(name, shape, dt))

        def bank(name):
            return ctx.enter_context(nc.psum_tensor(name, [P, 512], fp32))

        def sem(name):
            return ctx.enter_context(nc.semaphore(name))

        index = sb("index", [P, NT, NF], mybir.dt.int32)
        rows = sb("rows", [P, NT, NR, D])
        cols = sb("cols", [P, B, SP_])
        gram = sb("gram", [NS, NS - 1, P])
        flat = sb("flat", [P, NPAIR])
        pairs = sb("pairs", [PC, NC, P])
        w1d = sb("w1d", [P, 2, H1])
        w1s = sb("w1s", [P, H1])
        w1p = sb("w1p", [PC, NC, H1])
        w2s = sb("w2s", [P, K1, H2])
        w3s = sb("w3s", [P, K2])
        b1s = sb("b1s", [P, K1])
        b2s = sb("b2s", [P, K2])
        h1 = sb("h1", [P, K1, P])
        h2 = sb("h2", [P, K2, P])
        y = sb("y", [1, B])
        ident = sb("ident", [P, P])
        row_int = sb("row_int", [HP, HC], mybir.dt.int32)
        row_no = sb("row_no", [HP, HC])
        minus_row_no = sb("minus_row_no", [HP, HC])
        distance = sb("distance", [HP, HC - HV, B])
        hot_id = sb("hot_id", [P, NL, B], mybir.dt.int32)
        table = sb("table", [HP, NL, HC * D])
        table_hi = sb("table_hi", [HP, 2, HC * D], fp32r)
        table_lo = sb("table_lo", [HP, 2, HC * D], fp32r)
        hot = sb("hot", [HP, HC, B], fp32r)

        turn_ps = [bank("turn_ps0"), bank("turn_ps1")]
        gram_ps = [bank("gram_ps0"), bank("gram_ps1")]
        flat_ps = bank("flat_ps")
        h1_ps = [bank("h1_ps0"), bank("h1_ps1")]
        h2_ps = bank("h2_ps")

        ids_loaded = sem("ids_loaded")
        dense_loaded = sem("dense_loaded")
        w1d_loaded = sem("w1d_loaded")
        weights_loaded = sem("weights_loaded")
        half_loaded = sem("half_loaded")
        ids_0_loaded = sem("ids_0_loaded")
        table_loaded = [sem(f"table_loaded{n}") for n in range(NL)]
        gathered = [[sem(f"gathered{t}_{g}") for g in range(NG)] for t in range(NT)]
        ident_zeroed = sem("ident_zeroed")
        ident_ready = sem("ident_ready")
        row_counted = sem("row_counted")
        row_ready = sem("row_ready")
        pad_zeroed = sem("pad_zeroed")
        w1_summed = sem("w1_summed")
        hi_ready = sem("hi_ready")
        lo_ready = sem("lo_ready")
        hot_ready_v = sem("hot_ready_v")
        hot_ready_a = sem("hot_ready_a")
        far = sem("far")
        hot_used = sem("hot_used")
        hot_stored = sem("hot_stored")
        turned = sem("turned")
        stored = sem("stored")
        multiplied = sem("multiplied")
        picked_v = sem("picked_v")
        picked_a = sem("picked_a")
        flat_turned = sem("flat_turned")
        flat_stored_v = sem("flat_stored_v")
        flat_stored_a = sem("flat_stored_a")
        pairs_turned = sem("pairs_turned")
        pairs_stored = sem("pairs_stored")
        h1_summed = sem("h1_summed")
        h1_stored_a = sem("h1_stored_a")
        h1_stored_v = sem("h1_stored_v")
        h2_summed = sem("h2_summed")
        h2_stored_a = sem("h2_stored_a")
        h2_stored_v = sem("h2_stored_v")
        y_summed = sem("y_summed")
        y_stored = sem("y_stored")
        out_written = sem("out_written")

        block = ctx.enter_context(nc.Block())
        KH = K1 // 2
        NA = first_pair(JA)

        def h2_sums(m):
            return (h2_ps, flat_ps)[m][:, 0:P]

        def loads_of(k):
            return 3 * 16 * (k // NL + 1) - (16 if k % NL == 0 else 0)

        def pick_blocks(copy, t, q, quadrants):
            for s in quadrants:
                src = gram_ps[(t * NQ + q) % 2][SP_ * s:SP_ * s + NS, 0:GB * SB * (NS - 1)] \
                    .rearrange("p (k s j) -> p k s j", k=GB, s=SB)[:, :, s, :]
                first = q * GB * SB + s
                dst = gram[:, :, first:first + SB * (GB - 1) + 1:SB].rearrange("p j k -> p k j")
                last = copy(dst, src)
            return last

        @block.sync
        def _(sp):
            def load_ids(k, loaded):
                sp.dma_start(hot_id[:, k % NL, :], hot_ids[k:k + 1, :].to_broadcast([P, B])).then_inc(loaded, 16)

            def load_columns(k, first, end, loaded):
                src = tables[HOT[k]].rearrange("(p c) d -> p (c d)", c=HC)
                for p in (slice(0, HP16), slice(HP16, HP)):
                    sp.dma_start(table[p, k % NL, first:end], src[p, first:end]).then_inc(loaded, 16)

            def load_table(k):
                if k >= NL:
                    sp.wait_ge(lo_ready, k - NL + 1)
                    sp.wait_ge(hot_ready_v, (k - NL + 1) * HV)
                    sp.wait_ge(hot_ready_a, (k - NL + 1) * (HC - HV))
                load_ids(k, table_loaded[k % NL])
                load_columns(k, 0, HC * D, table_loaded[k % NL])

            sp.dma_start(index[:], ids.rearrange("(t p) f -> p t f", p=P)).then_inc(ids_loaded, 16)
            load_columns(0, 0, HC // 2 * D, half_loaded)
            load_ids(0, ids_0_loaded)
            load_columns(0, HC // 2 * D, HC * D, table_loaded[0])
            load_table(1)
            sp.dma_start(rows[:, :, 0, :], dense.rearrange("(t p) d -> p t d", p=P)).then_inc(dense_loaded, 16)
            for k in range(2, NH):
                load_table(k)
            sp.dma_start(w1d[:], w1_dense.rearrange("(a p) o -> p a o", p=P)).then_inc(w1d_loaded, 16)
            sp.dma_start(w1p[:], w1_pairs.rearrange("(c p) o -> p c o", p=PC)).then_inc(weights_loaded, 16)
            sp.dma_start(w2s[:], w2.rearrange("(k p) o -> p k o", p=P)).then_inc(weights_loaded, 16)
            sp.dma_start(w3s[:], w3).then_inc(weights_loaded, 16)
            sp.dma_start(b1s[:], b1).then_inc(weights_loaded, 16)
            sp.dma_start(b2s[:], b2).then_inc(weights_loaded, 16)
            sp.wait_ge(y_stored, NT)
            sp.dma_start(out.rearrange("b a -> a b"), y[:]).then_inc(out_written, 16)
            sp.wait_ge(out_written, 16)

        @block.gpsimd
        def _(pool):
            pool.iota(row_int[:], pattern=[[1, HC]], base=0, channel_multiplier=HC).then_inc(row_counted, 1)
            pool.memset(ident[:], 0.0).then_inc(ident_zeroed, 1)
            pool.wait_ge(ident_zeroed, 1)
            pool.affine_select(out=ident[:], in_=ident[:], compare_op=ALU.not_equal, fill=1.0, base=0,
                               pattern=[[-1, P]], channel_multiplier=1).then_inc(ident_ready, 1)
            pool.wait_ge(ids_loaded, 16)
            for t in range(NT):
                for n, f in enumerate(COLD):
                    pool.indirect_dma_start(rows[:, t, n + 1, :], None, tables[f],
                                            bass.IndirectOffsetOnAxis(index[:, t, f:f + 1], 0)) \
                        .then_inc(gathered[t][(n + 1) // GS], 16)

        @block.vector
        def _(dve):
            dve.wait_ge(row_counted, 1)
            nc.vector.tensor_copy(row_no[:], row_int[:]).then_inc(row_ready, 1)
            nc.vector.tensor_scalar(minus_row_no[:], row_int[:], -1.0, None, ALU.mult).then_inc(row_ready, 1)
            nc.vector.memset(cols[:, :, NS:SP_], 0.0).then_inc(pad_zeroed, 1)
            dve.wait_ge(row_ready, 1)

            def split_table(k):
                dve.wait_ge(table_loaded[k % NL], loads_of(k))
                dve.wait_ge(hi_ready, 2 * k + 2)
                if k >= 2:
                    dve.wait_ge(hot_used, (k - 1) * HC)
                nc.vector.tensor_tensor(table_lo[:, k % 2, :], table[:, k % NL, :], table_hi[:, k % 2, :],
                                        ALU.subtract).then_inc(lo_ready, 1)

            for k in range(NH):
                if k == 0:
                    dve.wait_ge(ids_0_loaded, 16)
                else:
                    dve.wait_ge(table_loaded[k % NL], loads_of(k))
                for c in range(HV):
                    if k >= 1:
                        dve.wait_ge(hot_used, (k - 1) * HC + c + 1)
                    nc.vector.tensor_scalar(hot[:, c, :], hot_id[0:HP, k % NL, :], row_no[:, c:c + 1], None,
                                            ALU.is_equal).then_inc(hot_ready_v, 1)
                    if k == 0 and c == HV - 1:
                        split_table(0)
                if k + 1 < NH:
                    split_table(k + 1)
            dve.wait_ge(w1d_loaded, 16)
            nc.vector.tensor_add(w1s[:], w1d[:, 0, :], w1d[:, 1, :]).then_inc(w1_summed, 1)
            dve.wait_ge(weights_loaded, 5 * 16)
            for t in range(NT):
                for q in range(NQ):
                    dve.wait_ge(multiplied, t * NQ + q + 1)
                    pick_blocks(nc.vector.tensor_copy, t, q, (0, 1)).then_inc(picked_v, 1)
                dve.wait_ge(flat_turned, 2 * t + 1)
                nc.vector.tensor_copy(flat[:, 0:NA], flat_ps[:, 0:NA]).then_inc(flat_stored_v, 1)
                dve.wait_ge(pairs_turned, 2 * t + 1)
                nc.vector.tensor_copy(pairs[:, 0, :], flat_ps[0:PC, 0:P]).then_inc(pairs_stored, 1)
                dve.wait_ge(pairs_turned, 2 * t + 2)
                nc.vector.tensor_copy(pairs[:, 1:NC, :], h2_ps[0:PC, 0:(NC - 1) * P].rearrange("p (c b) -> p c b", b=P)) \
                    .then_inc(pairs_stored, 1)
                dve.wait_ge(h1_summed, 2 * t + 2)
                for k in range(KH, K1):
                    last = nc.vector.tensor_scalar(h1[:, k, :], h1_ps[1][:, (k - KH) * P:(k - KH + 1) * P],
                                                   b1s[:, k:k + 1], 0.0, ALU.add, ALU.max)
                last.then_inc(h1_stored_v, 1)
                dve.wait_ge(h2_summed, 2 * t + 2)
                nc.vector.tensor_scalar(h2[:, 1, :], h2_sums(1), b2s[:, 1:2], 0.0, ALU.add, ALU.max) \
                    .then_inc(h2_stored_v, 1)

        @block.scalar
        def _(act):
            def store_group(t, g):
                n = t * NG + g
                slots = group_slots(g)
                k = len(slots)
                act.wait_ge(turned, n + 1)
                nc.scalar.copy(cols[:, t * P:(t + 1) * P, slots[0]:slots[0] + k],
                               turn_ps[n % 2][:, 0:k * P].rearrange("p (s b) -> p b s", s=k)).then_inc(stored, 1)

            def store_hot(k):
                act.wait_ge(hot_used, (k + 1) * HC)
                nc.scalar.copy(cols[:, :, NR + k], h1_ps[k % 2][:]).then_inc(hot_stored, 1)

            def round_table(k):
                if k > 0:
                    act.wait_ge(table_loaded[k % NL], loads_of(k))
                if k >= 2:
                    act.wait_ge(hot_used, (k - 1) * HC)
                for h in range(2):
                    if k == 0:
                        act.wait_ge((half_loaded, table_loaded[0])[h], 2 * 16)
                    half = slice(h * HC // 2 * D, (h + 1) * HC // 2 * D)
                    nc.scalar.copy(table_hi[:, k % 2, half], table[:, k % NL, half]).then_inc(hi_ready, 1)

            def store_flat(t):
                act.wait_ge(flat_turned, 2 * t + 2)
                nc.scalar.copy(flat[:, NA:NPAIR], h2_ps[:, 0:NPAIR - NA]).then_inc(flat_stored_a, 1)

            def store_h1(t):
                act.wait_ge(h1_summed, 2 * t + 1)
                if t == 0:
                    act.wait_ge(weights_loaded, 5 * 16)
                for k in range(KH):
                    last = nc.scalar.activation(h1[:, k, :], h1_ps[0][:, k * P:(k + 1) * P], ACT.Relu,
                                                bias=b1s[:, k:k + 1])
                last.then_inc(h1_stored_a, 1)

            def store_h2(t):
                act.wait_ge(h2_summed, 2 * t + 1)
                nc.scalar.activation(h2[:, 0, :], h2_sums(0), ACT.Relu, bias=b2s[:, 0:1]).then_inc(h2_stored_a, 1)

            def store_y(t):
                act.wait_ge(y_summed, t + 1)
                nc.scalar.copy(y[0:1, t * P:(t + 1) * P], h2_ps[0:1, P:2 * P]).then_inc(y_stored, 1)

            def make_hot(k):
                for c in range(HV, HC):
                    if k >= 1:
                        act.wait_ge(hot_ready_a, k * (HC - HV))
                    nc.scalar.activation(distance[:, c - HV, :], hot_id[0:HP, k % NL, :], ACT.Abs,
                                         bias=minus_row_no[:, c:c + 1]).then_inc(far, 1)
                for c in range(HV, HC):
                    act.wait_ge(far, k * (HC - HV) + c - HV + 1)
                    if k >= 1:
                        act.wait_ge(hot_used, (k - 1) * HC + c + 1)
                    nc.scalar.activation(hot[:, c, :], distance[:, c - HV, :], ACT.Relu, bias=1.0, scale=-1.0) \
                        .then_inc(hot_ready_a, 1)

            round_table(0)
            act.wait_ge(row_ready, 2)
            act.wait_ge(ids_0_loaded, 16)
            make_hot(0)
            round_table(1)
            for k in range(1, NH + 1):
                if k + 1 < NH:
                    round_table(k + 1)
                if k < NH:
                    make_hot(k)
                store_hot(k - 1)
                for g in first_turns(k - 1):
                    store_group(0, g)
            for t in range(NT + 1):
                if t >= 1:
                    if t < NT:
                        store_group(t, 0)
                    store_flat(t - 1)
                    if t < NT:
                        store_group(t, 1)
                    store_h1(t - 1)
                    if t < NT:
                        store_group(t, 2)
                    store_h2(t - 1)
                    if t < NT:
                        for g in range(3, NG):
                            store_group(t, g)
                    store_y(t - 1)
                if t < NT:
                    for q in range(NQ):
                        act.wait_ge(multiplied, t * NQ + q + 1)
                        pick_blocks(nc.scalar.copy, t, q, (2, 3)).then_inc(picked_a, 1)

        @block.tensor
        def _(pe):
            def look_up(k):
                if k >= 2:
                    pe.wait_ge(hot_stored, k - 1)
                order = [(c, part) for part in range(2) for c in range(HC)] if k == 0 else \
                    [(c, part) for c in range(HC) for part in range(2)]
                for n, (c, part) in enumerate(order):
                    if part == 0 and c % (HC // 2) == 0:
                        pe.wait_ge(hi_ready, 2 * k + 1 + c // (HC // 2))
                    if part == 0 and c < HV:
                        pe.wait_ge(hot_ready_v, k * HV + c + 1)
                    elif part == 0:
                        pe.wait_ge(hot_ready_a, k * (HC - HV) + c - HV + 1)
                    elif c == 0:
                        pe.wait_ge(lo_ready, k + 1)
                    last = nc.tensor.matmul(h1_ps[k % 2][:], (table_hi, table_lo)[part][:, k % 2, c * D:(c + 1) * D],
                                            hot[:, c, :], start=n == 0, stop=n == 2 * HC - 1)
                    if part == 1:
                        last.then_inc(hot_used, 1)

            def turn_group(t, g):
                n = t * NG + g
                slots = group_slots(g)
                if n == 0:
                    pe.wait_ge(dense_loaded, 16)
                pe.wait_ge(gathered[t][g], 16 * sum(s > 0 for s in slots))
                if n >= 2:
                    pe.wait_ge(stored, n - 1)
                for k, s in enumerate(slots):
                    last = nc.tensor.transpose(turn_ps[n % 2][:, k * P:(k + 1) * P], rows[:, t, s, :], ident[:])
                last.then_inc(turned, 1)

            def multiply(t):
                pe.wait_ge(stored, (t + 1) * NG)
                if t == 0:
                    pe.wait_ge(hot_stored, NH)
                    pe.wait_ge(pad_zeroed, 1)
                for q in range(NQ):
                    m = t * NQ + q
                    if m >= 2:
                        pe.wait_ge(picked_v, m - 1)
                        pe.wait_ge(picked_a, m - 1)
                    for k in range(GB):
                        b = t * P + (q * GB + k) * SB
                        last = nc.tensor.matmul(gram_ps[m % 2][:, k * SB * (NS - 1):(k + 1) * SB * (NS - 1)],
                                                cols[:, b:b + SB, :], cols[:, b:b + SB, 1:NS], start=True, stop=True)
                    last.then_inc(multiplied, 1)

            def flatten(t):
                pe.wait_ge(picked_v, (t + 1) * NQ)
                pe.wait_ge(picked_a, (t + 1) * NQ)
                if t >= 1:
                    pe.wait_ge(h2_stored_v, t)
                    pe.wait_ge(y_stored, t)
                for j in range(1, NS):
                    at = first_pair(j) if j < JA else first_pair(j) - NA
                    last = nc.tensor.transpose((flat_ps if j < JA else h2_ps)[:, at:at + j], gram[0:j, j - 1, :],
                                               ident[0:j, 0:j])
                    if j in (JA - 1, NS - 1):
                        last.then_inc(flat_turned, 1)

            def turn_pairs(t, chunks):
                pe.wait_ge(flat_stored_v, t + 1) if chunks[0] == 0 else pe.wait_ge(flat_stored_a, t + 1)
                for c in chunks:
                    into = flat_ps[0:PC, 0:P] if c == 0 else h2_ps[0:PC, (c - 1) * P:c * P]
                    last = nc.tensor.transpose(into, flat[:, c * PC:(c + 1) * PC], ident[:])
                last.then_inc(pairs_turned, 1)

            def h1_sums(k):
                return h1_ps[k // KH][:, k % KH * P:(k % KH + 1) * P]

            def layer_1_dense(t, half):
                if t == 0:
                    pe.wait_ge(w1_summed, 1)
                    pe.wait_ge(hot_stored, NH - (NH - 1 - half) % 2)
                    pe.wait_ge(stored, 1)
                else:
                    pe.wait_ge((h1_stored_a, h1_stored_v)[half], t)
                for k in range(KH * half, KH * half + KH):
                    nc.tensor.matmul(h1_sums(k), w1s[:, k * P:(k + 1) * P], cols[:, t * P:(t + 1) * P, 0],
                                     start=k % KH == 0, stop=False, skip_group_check=True)

            def layer_1(t):
                if t == 0:
                    pe.wait_ge(weights_loaded, 5 * 16)
                pe.wait_ge(pairs_stored, 2 * t + 1)
                for k in range(K1):
                    nc.tensor.matmul(h1_sums(k), w1p[:, 0, k * P:(k + 1) * P], pairs[:, 0, :],
                                     start=False, stop=False, skip_group_check=True)
                pe.wait_ge(pairs_stored, 2 * t + 2)
                for half in range(2):
                    for c in range(1, NC):
                        for k in range(KH * half, KH * half + KH):
                            last = nc.tensor.matmul(h1_sums(k), w1p[:, c, k * P:(k + 1) * P], pairs[:, c, :],
                                                    start=False, stop=c == NC - 1, skip_group_check=True)
                    last.then_inc(h1_summed, 1)

            def layer_2(t):
                pe.wait_ge(h1_stored_a, t + 1)
                if t >= 1:
                    pe.wait_ge(y_stored, t)
                for half in range(2):
                    if half == 1:
                        pe.wait_ge(h1_stored_v, t + 1)
                    for m in range(K2):
                        for k in range(KH * half, KH * half + KH):
                            last = nc.tensor.matmul(h2_sums(m), w2s[:, k, m * P:(m + 1) * P], h1[:, k, :],
                                                    start=k == 0, stop=k == K1 - 1)
                        if half == 1:
                            last.then_inc(h2_summed, 1)

            def layer_3(t):
                for k in range(K2):
                    pe.wait_ge((h2_stored_a, h2_stored_v)[k], t + 1)
                    last = nc.tensor.matmul(h2_ps[0:1, P:2 * P], w3s[:, k:k + 1], h2[:, k, :],
                                            start=k == 0, stop=k == K2 - 1)
                last.then_inc(y_summed, 1)

            for k in range(NH):
                look_up(k)
                if k == 0:
                    pe.wait_ge(ident_ready, 1)
                for g in first_turns(k):
                    turn_group(0, g)
            for t in range(NT + 1):
                if t >= 1:
                    if t < NT:
                        turn_group(t, 0)
                    layer_1_dense(t - 1, 0)
                    flatten(t - 1)
                    if t < NT:
                        turn_group(t, 1)
                    turn_pairs(t - 1, (0,))
                    turn_pairs(t - 1, (1, 2))
                    layer_1(t - 1)
                    if t < NT:
                        turn_group(t, 2)
                    layer_2(t - 1)
                    if t < NT:
                        for g in range(3, NG):
                            turn_group(t, g)
                    layer_3(t - 1)
                if t < NT:
                    layer_1_dense(t, 1)
                if t < NT:
                    multiply(t)


def kernel(**inputs):
    import numpy as np
    import concourse.bacc as bacc
    from concourse.bass_utils import run_bass_kernel_spmd as run

    nc = bacc.Bacc("TRN2", target_bir_lowering=False, num_devices=1)
    arrays = {}

    def given(name, a):
        arrays[name] = np.ascontiguousarray(a)
        return nc.dram_tensor(name, arrays[name].shape, mybir.dt.from_np(arrays[name].dtype),
                              kind="ExternalInput").ap()

    w1 = np.asarray(inputs["W_top1"])
    pair_at = D + np.array(pair_rows())
    args = [
        given("dense", inputs["r_dense_features"]),
        given("ids", inputs["ids"]),
        given("hot_ids", np.asarray(inputs["ids"])[:, HOT].T),
        [given(f"tbl_{f}", inputs[f"tbl_{f}"]) for f in range(NF)],
        given("w1_dense", np.concatenate([w1[:D], w1[D + NPAIR:]])),
        given("w1_pairs", w1[pair_at]),
        given("b1", np.asarray(inputs["b_top1"]).reshape(K1, P).T),
        given("w2", inputs["W_top2"]),
        given("b2", np.asarray(inputs["b_top2"]).reshape(K2, P).T),
        given("w3", np.asarray(inputs["W_top3"]).reshape(K2, P).T),
    ]
    out = nc.dram_tensor("out", (B, 1), mybir.dt.float32, kind="ExternalOutput").ap()
    dlrm_tower(nc, *args, out)
    result = run(nc, [arrays], core_ids=[0])
    return result.results[0]["out"]
```
